# Optimizing a Trainium2 kernel written in Bass

```python
import numpy as np
import jax
import jax.numpy as jnp

def _softmax(x, axis=-1):
    return jax.nn.softmax(x, axis=axis)

def _gelu(x):
    return jax.nn.gelu(x, approximate=True)

def _silu(x):
    return jax.nn.silu(x)

def _sigmoid(x):
    return jax.nn.sigmoid(x)

def _layernorm(x, axis=-1, eps=1e-05):
    m = jnp.mean(x, axis=axis, keepdims=True)
    v = jnp.var(x, axis=axis, keepdims=True)
    return (x - m) / jnp.sqrt(v + eps)

def _scatter_add(tgt, idx, src, axis=0):
    return tgt.at[idx].add(src)

def _segment_sum(src, seg, n):
    return jax.ops.segment_sum(src, seg, n)
kernel_name = 'mk_dlrm_tower_d1_rec_r8_eab25d'

def setup_inputs(seed: int=0):
    np.random.seed(seed)
    _w = jnp.asarray

    def _rec_inputs():
        import jax
        import jax.numpy as jnp
        _tk = jax.random.key(seed)
        ids = jnp.stack([jax.random.randint(jax.random.fold_in(_tk, 200 + f), (512,), 0, v, jnp.int32) for f, v in enumerate([12500, 1000, 1250, 12500, 125000, 1250, 12500, 1250, 1000, 1250, 1000, 1250, 12500, 1000, 12500, 12500, 1000, 1250, 1000, 1250, 12500, 12500, 1000, 1250, 1250, 1250])], axis=1)
        tbl_0 = 0.05 * jax.random.normal(jax.random.fold_in(_tk, 500 + 0), (12500, 128), jnp.float32)
        tbl_1 = 0.05 * jax.random.normal(jax.random.fold_in(_tk, 500 + 1), (1000, 128), jnp.float32)
        tbl_2 = 0.05 * jax.random.normal(jax.random.fold_in(_tk, 500 + 2), (1250, 128), jnp.float32)
        tbl_3 = 0.05 * jax.random.normal(jax.random.fold_in(_tk, 500 + 3), (12500, 128), jnp.float32)
        tbl_4 = 0.05 * jax.random.normal(jax.random.fold_in(_tk, 500 + 4), (125000, 128), jnp.float32)
        tbl_5 = 0.05 * jax.random.normal(jax.random.fold_in(_tk, 500 + 5), (1250, 128), jnp.float32)
        tbl_6 = 0.05 * jax.random.normal(jax.random.fold_in(_tk, 500 + 6), (12500, 128), jnp.float32)
        tbl_7 = 0.05 * jax.random.normal(jax.random.fold_in(_tk, 500 + 7), (1250, 128), jnp.float32)
        tbl_8 = 0.05 * jax.random.normal(jax.random.fold_in(_tk, 500 + 8), (1000, 128), jnp.float32)
        tbl_9 = 0.05 * jax.random.normal(jax.random.fold_in(_tk, 500 + 9), (1250, 128), jnp.float32)
        tbl_10 = 0.05 * jax.random.normal(jax.random.fold_in(_tk, 500 + 10), (1000, 128), jnp.float32)
        tbl_11 = 0.05 * jax.random.normal(jax.random.fold_in(_tk, 500 + 11), (1250, 128), jnp.float32)
        tbl_12 = 0.05 * jax.random.normal(jax.random.fold_in(_tk, 500 + 12), (12500, 128), jnp.float32)
        tbl_13 = 0.05 * jax.random.normal(jax.random.fold_in(_tk, 500 + 13), (1000, 128), jnp.float32)
        tbl_14 = 0.05 * jax.random.normal(jax.random.fold_in(_tk, 500 + 14), (12500, 128), jnp.float32)
        tbl_15 = 0.05 * jax.random.normal(jax.random.fold_in(_tk, 500 + 15), (12500, 128), jnp.float32)
        tbl_16 = 0.05 * jax.random.normal(jax.random.fold_in(_tk, 500 + 16), (1000, 128), jnp.float32)
        tbl_17 = 0.05 * jax.random.normal(jax.random.fold_in(_tk, 500 + 17), (1250, 128), jnp.float32)
        tbl_18 = 0.05 * jax.random.normal(jax.random.fold_in(_tk, 500 + 18), (1000, 128), jnp.float32)
        tbl_19 = 0.05 * jax.random.normal(jax.random.fold_in(_tk, 500 + 19), (1250, 128), jnp.float32)
        tbl_20 = 0.05 * jax.random.normal(jax.random.fold_in(_tk, 500 + 20), (12500, 128), jnp.float32)
        tbl_21 = 0.05 * jax.random.normal(jax.random.fold_in(_tk, 500 + 21), (12500, 128), jnp.float32)
        tbl_22 = 0.05 * jax.random.normal(jax.random.fold_in(_tk, 500 + 22), (1000, 128), jnp.float32)
        tbl_23 = 0.05 * jax.random.normal(jax.random.fold_in(_tk, 500 + 23), (1250, 128), jnp.float32)
        tbl_24 = 0.05 * jax.random.normal(jax.random.fold_in(_tk, 500 + 24), (1250, 128), jnp.float32)
        tbl_25 = 0.05 * jax.random.normal(jax.random.fold_in(_tk, 500 + 25), (1250, 128), jnp.float32)
        _rk = jax.random.fold_in(_tk, 7)
        r_dense_features = -0.000520686 + 1.00062 * jax.random.normal(jax.random.fold_in(_rk, 101), (512, 128), jnp.float32)
        W_top1 = 0.0405887 * jax.random.normal(jax.random.fold_in(_tk, 801), (607, 512), jnp.float32)
        W_top2 = 0.0441942 * jax.random.normal(jax.random.fold_in(_tk, 802), (512, 256), jnp.float32)
        W_top3 = 0.0625 * jax.random.normal(jax.random.fold_in(_tk, 803), (256, 1), jnp.float32)
        b_top1 = jnp.zeros((512,), jnp.float32)
        b_top2 = jnp.zeros((256,), jnp.float32)
        return (r_dense_features, ids, tbl_0, tbl_1, tbl_2, tbl_3, tbl_4, tbl_5, tbl_6, tbl_7, tbl_8, tbl_9, tbl_10, tbl_11, tbl_12, tbl_13, tbl_14, tbl_15, tbl_16, tbl_17, tbl_18, tbl_19, tbl_20, tbl_21, tbl_22, tbl_23, tbl_24, tbl_25, W_top1, b_top1, W_top2, b_top2, W_top3)
    r_dense_features, ids, tbl_0, tbl_1, tbl_2, tbl_3, tbl_4, tbl_5, tbl_6, tbl_7, tbl_8, tbl_9, tbl_10, tbl_11, tbl_12, tbl_13, tbl_14, tbl_15, tbl_16, tbl_17, tbl_18, tbl_19, tbl_20, tbl_21, tbl_22, tbl_23, tbl_24, tbl_25, W_top1, b_top1, W_top2, b_top2, W_top3 = _rec_inputs()

    def _L0_rec_setup():
        import jax, jax.numpy as jnp
        import numpy as np
        B, F, D = (2048, 26, 128)
        key = jax.random.key(seed)
        k1, k2 = jax.random.split(key)
        dense_features = jax.random.normal(k1, (B, D), dtype=jnp.float32)
        sparse_values = jax.random.normal(k2, (B, F, D), dtype=jnp.float32)
        return {'dense_features': dense_features, 'sparse_values': sparse_values}
    _L0_rec_all = _L0_rec_setup()
    _L0_rec_in = {k: v for k, v in _L0_rec_all.items() if k in ()}
    del _L0_rec_all
    return {'r_dense_features': r_dense_features, 'ids': ids, 'tbl_0': tbl_0, 'tbl_1': tbl_1, 'tbl_2': tbl_2, 'tbl_3': tbl_3, 'tbl_4': tbl_4, 'tbl_5': tbl_5, 'tbl_6': tbl_6, 'tbl_7': tbl_7, 'tbl_8': tbl_8, 'tbl_9': tbl_9, 'tbl_10': tbl_10, 'tbl_11': tbl_11, 'tbl_12': tbl_12, 'tbl_13': tbl_13, 'tbl_14': tbl_14, 'tbl_15': tbl_15, 'tbl_16': tbl_16, 'tbl_17': tbl_17, 'tbl_18': tbl_18, 'tbl_19': tbl_19, 'tbl_20': tbl_20, 'tbl_21': tbl_21, 'tbl_22': tbl_22, 'tbl_23': tbl_23, 'tbl_24': tbl_24, 'tbl_25': tbl_25, 'W_top1': W_top1, 'b_top1': b_top1, 'W_top2': W_top2, 'b_top2': b_top2, 'W_top3': W_top3}

def reference(r_dense_features, ids, tbl_0, tbl_1, tbl_2, tbl_3, tbl_4, tbl_5, tbl_6, tbl_7, tbl_8, tbl_9, tbl_10, tbl_11, tbl_12, tbl_13, tbl_14, tbl_15, tbl_16, tbl_17, tbl_18, tbl_19, tbl_20, tbl_21, tbl_22, tbl_23, tbl_24, tbl_25, W_top1, b_top1, W_top2, b_top2, W_top3):
    import jax
    import jax.numpy as jnp

    def _L0_rec_ref(dense_features, sparse_values):
        import jax, jax.numpy as jnp
        import numpy as np
        B, F, D = (2048, 26, 128)
        sd = jnp.einsum('bfd,bd->bf', sparse_values, dense_features)
        ss = jnp.einsum('bfd,bgd->bfg', sparse_values, sparse_values)
        iu, ju = jnp.triu_indices(F, k=1)
        pairs = ss[:, iu, ju]
        return jnp.concatenate([dense_features, sd, pairs], axis=1)
    e = jnp.stack([tbl_0[ids[:, 0]], tbl_1[ids[:, 1]], tbl_2[ids[:, 2]], tbl_3[ids[:, 3]], tbl_4[ids[:, 4]], tbl_5[ids[:, 5]], tbl_6[ids[:, 6]], tbl_7[ids[:, 7]], tbl_8[ids[:, 8]], tbl_9[ids[:, 9]], tbl_10[ids[:, 10]], tbl_11[ids[:, 11]], tbl_12[ids[:, 12]], tbl_13[ids[:, 13]], tbl_14[ids[:, 14]], tbl_15[ids[:, 15]], tbl_16[ids[:, 16]], tbl_17[ids[:, 17]], tbl_18[ids[:, 18]], tbl_19[ids[:, 19]], tbl_20[ids[:, 20]], tbl_21[ids[:, 21]], tbl_22[ids[:, 22]], tbl_23[ids[:, 23]], tbl_24[ids[:, 24]], tbl_25[ids[:, 25]]], axis=1)
    z = _L0_rec_ref(r_dense_features, e)
    z = z.reshape(z.shape[0], -1)
    h = jnp.concatenate([z, r_dense_features], axis=1)
    h = jnp.maximum(h @ W_top1 + b_top1, 0.0)
    h = jnp.maximum(h @ W_top2 + b_top2, 0.0)
    y = h @ W_top3
    return y

_drawn_inputs = setup_inputs


def setup_inputs(seed=0):
    import zlib

    import numpy as np

    out = dict(_drawn_inputs(seed))
    spreads = {'b_top1': (0.0, 0.1), 'b_top2': (0.0, 0.1)}
    factors = {}
    for name, (base, spread) in spreads.items():
        noise = np.random.default_rng([zlib.crc32(name.encode()), seed]).standard_normal(out[name].shape)
        drawn = base * np.exp(spread * noise) if base else spread * noise
        out[name] = jnp.asarray(drawn.astype(out[name].dtype))
    for name, factor in factors.items():
        out[name] = (out[name] * factor).astype(out[name].dtype)
    return out
```

```python
from contextlib import ExitStack

import concourse.bass as bass
from concourse import mybir

ALU = mybir.AluOpType
ACT = mybir.ActivationFunctionType
F32 = mybir.dt.float32
U32 = mybir.dt.uint32

P = 128
QUAD = 32


def dlrm_tower_kernel(nc, dense, ids, tables, W1, b1, W2, b2, W3, out):
    B, D = dense.shape
    F = ids.shape[1]
    NV = F + 1
    NT = B // P
    N1 = W1.shape[1]
    N2 = W2.shape[1]
    N1T, N2T = N1 // P, N2 // P
    NC = NV - 1
    SLOTS = -(-NC // 4)
    COL0 = [min(k * SLOTS, NC - SLOTS) for k in range(4)]
    TPG = 4
    NG = -(-NV // TPG)
    GS = 4
    CH = 32
    NCH = P // CH
    BG = CH // GS // 2
    assert D == P and B % (2 * P) == 0 and N1T == 4 and N2T == 2 and NG % 2 == 1

    dense_t = dense.rearrange("(p t) d -> p t d", t=NT)
    ids_t = ids.bitcast(U32).rearrange("(p t) f -> p t f", t=NT)

    with ExitStack() as ctx:
        def sb(name, shape, dt=F32):
            return ctx.enter_context(nc.sbuf_tensor(name, shape, dt))

        def psum(name, shape):
            return ctx.enter_context(nc.psum_tensor(name, shape, F32))

        def sem(name):
            return ctx.enter_context(nc.semaphore(name))

        ident = sb("ident", [P, P])
        idx = sb("idx", [P, 2, F], U32)
        vecs = sb("vecs", [P, 2, NV, D])
        vecsT = sb("vecsT", [P, 2, P, QUAD])
        denseT = sb("denseT", [P, 2, P])
        Z = sb("Z", [P, SLOTS, P])
        Wz = sb("Wz", [P, SLOTS, N1])
        Wda = sb("Wda", [P, N1])
        Wdb = sb("Wdb", [P, N1])
        Wd = sb("Wd", [P, N1])
        W2s = sb("W2s", [P, N1T, N2])
        rows = sb("rows", [N1T + 2 * N2T, P])
        cols = sb("cols", [P, N1T + 2 * N2T])
        h1 = sb("h1", [P, N1T, P])
        h2 = sb("h2", [P, N2T, P])
        y = sb("y", [1, P, NT])

        tpb = psum("tpb", [P, 2, TPG * P])
        gram = psum("gram", [P, 2, 2, 512])
        mlp = psum("mlp", [P, 2, 512])

        ids_loaded = [sem(f"ids_loaded{s}") for s in range(2)]
        dense_loaded = [sem(f"dense_loaded{s}") for s in range(2)]
        gathered = [[sem(f"gathered{s}_{g}") for g in range(NG)] for s in range(2)]
        ident_zero = sem("ident_zero")
        ident_ready = sem("ident_ready")
        wz_zeroed = sem("wz_zeroed")
        wz_loaded = sem("wz_loaded")
        wd_loaded = sem("wd_loaded")
        wd_ready = sem("wd_ready")
        w2_loaded = sem("w2_loaded")
        rows_loaded = sem("rows_loaded")
        cols_psum = sem("cols_psum")
        tile_transposed = sem("tile_transposed")
        tp_full = [sem("tp_full0"), sem("tp_full1")]
        tp_free = [sem("tp_free0"), sem("tp_free1")]
        gram_full = sem("gram_full")
        gram_copied = [sem("gram_copied0"), sem("gram_copied1")]
        l1_full = [sem("l1_full0"), sem("l1_full1")]
        h1_ready = [sem("h1_ready0"), sem("h1_ready1")]
        l2_full = [sem("l2_full0"), sem("l2_full1")]
        h2_ready = [sem("h2_ready0"), sem("h2_ready1")]
        l3_full = sem("l3_full")
        mlp_free = sem("mlp_free")
        y_stored = sem("y_stored")

        block = ctx.enter_context(nc.Block())

        def group(g):
            return range(TPG * g, min(TPG * g + TPG, NV))

        @block.sync
        def _(sp):
            def load_tile(t, s):
                sp.dma_start(idx[:, s, :], ids_t[:, t, :]).then_inc(ids_loaded[s], 16)
                sp.dma_start(vecs[:, s, 0, :], dense_t[:, t, :]).then_inc(dense_loaded[s], 16)

            load_tile(0, 0)
            sp.dma_start(rows[0:N1T, :], b1.rearrange("(n p) -> n p", p=P)).then_inc(rows_loaded, 16)
            sp.dma_start(rows[N1T:N1T + N2T, :], b2.rearrange("(n p) -> n p", p=P)).then_inc(rows_loaded, 16)
            sp.dma_start(rows[N1T + N2T:N1T + 2 * N2T, :],
                         W3.rearrange("(n p) o -> n (p o)", p=P)).then_inc(rows_loaded, 16)
            load_tile(1, 1)
            sp.dma_start(Wda[:], W1[0:D, :]).then_inc(wd_loaded, 16)
            sp.dma_start(Wdb[:], W1[W1.shape[0] - D:W1.shape[0], :]).then_inc(wd_loaded, 16)
            sp.wait_ge(wz_zeroed, 1)
            row = D
            for c in range(NC):
                k = min(c // SLOTS, 3)
                n = NC - c
                sp.dma_start(Wz[QUAD * k + c + 1:QUAD * k + c + 1 + n, c - COL0[k], :],
                             W1[row:row + n, :]).then_inc(wz_loaded, 16)
                row += n
            sp.dma_start(W2s[:], W2.rearrange("(k p) n -> p k n", p=P)).then_inc(w2_loaded, 16)
            with sp.Fori(1, NT // 2) as i:
                for s in range(2):
                    sp.wait_ge(tile_transposed, 2 * i + s - 1)
                    load_tile(2 * i + s, s)
            sp.wait_ge(mlp_free, NT + 1)
            sp.dma_start(out.rearrange("b o -> o b"), y[:].rearrange("o p t -> o (p t)")).then_inc(y_stored, 16)
            sp.wait_ge(y_stored, 16)

        @block.gpsimd
        def _(pool):
            nc.gpsimd.memset(ident[:], 0.0).then_inc(ident_zero, 1)
            pool.wait_ge(ident_zero, 1)
            nc.gpsimd.affine_select(out=ident[:], in_=ident[:], compare_op=ALU.not_equal, fill=1.0, base=0,
                                    pattern=[[-1, P]], channel_multiplier=1).then_inc(ident_ready, 1)

            def gather(s):
                for g in range(NG):
                    for v in group(g):
                        if v:
                            nc.gpsimd.indirect_dma_start(
                                vecs[:, s, v, :], None, tables[v - 1],
                                bass.IndirectOffsetOnAxis(idx[:, s, v - 1:v], 0)).then_inc(gathered[s][g], 16)

            for s in range(2):
                pool.wait_ge(ids_loaded[s], 16)
                gather(s)
            with pool.Fori(1, NT // 2) as i:
                for s in range(2):
                    pool.wait_ge(tile_transposed, 2 * i + s - 1)
                    pool.wait_ge(ids_loaded[s], 16 * (i + 1))
                    gather(s)

        def copy_out(e, eng, copy, relu):

            def transposes(i, s):
                for g in range(NG):
                    if (NG * s + g) % 2 != e:
                        continue
                    m = (NG * s + g) // 2
                    eng.wait_ge(tp_full[e], NG * i + m + 1)
                    v0, nv = TPG * g, len(group(g))
                    src = tpb[:, e, 0:nv * P].rearrange("d (v b) -> d b v", v=nv)
                    if g == 0:
                        copy(denseT[:, s, :], tpb[:, e, 0:P])
                    copy(vecsT[:, s, :, v0:v0 + nv], src).then_inc(tp_free[e], 1)

            def products(i, s):
                for ch in range(NCH):
                    eng.wait_ge(gram_full, NCH * (2 * i + s) + ch + 1)
                    for j in (2 * e, 2 * e + 1):
                        for k in range(4):
                            src = gram[QUAD * j:QUAD * (j + 1), ch % 2, :, 0:BG * GS * NC].rearrange(
                                "r a (q j c) -> r j a q c", q=BG, j=GS)[:, j, :, :, COL0[k]:COL0[k] + SLOTS]
                            dst = Z[QUAD * k:QUAD * (k + 1), :, CH * ch:CH * (ch + 1)].rearrange(
                                "r c (a q j) -> r j a q c", q=BG, j=GS)[:, j]
                            last = copy(dst, src)
                    last.then_inc(gram_copied[e], 1)

            def layers(i, s):
                eng.wait_ge(l1_full[e], 2 * i + s + 1)
                for n in (2 * e, 2 * e + 1):
                    last = relu(h1[:, n, :], mlp[:, e, (n % 2) * P:(n % 2 + 1) * P], cols[:, n:n + 1])
                last.then_inc(h1_ready[e], 1)
                eng.wait_ge(l2_full[e], 2 * i + s + 1)
                relu(h2[:, e, :], mlp[:, e, 0:P], cols[:, N1T + e:N1T + e + 1]).then_inc(h2_ready[e], 1)

            return transposes, products, layers

        @block.vector
        def _(dve):
            for e in range(2):
                nc.vector.memset(vecsT[:, e, :, NV:QUAD], 0.0).then_inc(tp_free[e], 1)
            nc.vector.memset(Wz[:], 0.0).then_inc(wz_zeroed, 1)
            dve.wait_ge(cols_psum, 1)
            nc.vector.tensor_copy(cols[:], mlp[:, 0, 0:N1T + 2 * N2T]).then_inc(mlp_free, 1)
            dve.wait_ge(wd_loaded, 32)
            nc.vector.tensor_tensor(Wd[:], Wda[:], Wdb[:], ALU.add).then_inc(wd_ready, 1)
            dve.wait_ge(mlp_free, 1)

            def relu(dst, src, bias):
                return nc.vector.tensor_scalar(dst, src, bias, 0.0, ALU.add, ALU.max)

            transposes, products, layers = copy_out(0, dve, nc.vector.tensor_copy, relu)
            with dve.Fori(0, NT // 2) as i:
                for s in range(2):
                    transposes(i, s)
                    products(i, s)
                    layers(i, s)
                    dve.wait_ge(l3_full, 2 * i + s + 1)
                    nc.vector.tensor_copy(y[:, :, bass.ds(2 * i + s, 1)].rearrange("o p t -> o (p t)"),
                                          mlp[0:1, 0, 0:P]).then_inc(mlp_free, 1)

        @block.scalar
        def _(act):
            act.wait_ge(mlp_free, 1)

            def relu(dst, src, bias):
                return nc.scalar.activation(dst, src, ACT.Relu, bias=bias)

            transposes, products, layers = copy_out(1, act, nc.scalar.copy, relu)
            with act.Fori(0, NT // 2) as i:
                for s in range(2):
                    transposes(i, s)
                    products(i, s)
                    layers(i, s)

        @block.tensor
        def _(pe):
            pe.wait_ge(ident_ready, 1)
            pe.wait_ge(rows_loaded, 48)
            nr = N1T + 2 * N2T
            nc.tensor.transpose(mlp[:, 0, 0:nr], rows[:], ident[0:nr, 0:nr]).then_inc(cols_psum, 1)

            def tile(i, s):
                t = 2 * i + s
                pe.wait_ge(dense_loaded[s], 16 * (i + 1))
                for g in range(NG):
                    e = (NG * s + g) % 2
                    pe.wait_ge(tp_free[e], NG * i + (NG * s + g) // 2 + 1)
                    pe.wait_ge(gathered[s][g], 16 * (len(group(g)) - (g == 0)) * (i + 1))
                    for v in group(g):
                        last = nc.tensor.transpose(tpb[:, e, (v % TPG) * P:(v % TPG + 1) * P],
                                                   vecs[:, s, v, :], ident[:])
                    last.then_inc(tp_full[e], 1)

                done = NG * (s + 1)
                pe.wait_ge(tp_free[0], NG * i + (done + 1) // 2 + 1)
                pe.wait_ge(tp_free[1], NG * i + done // 2 + 1)
                for ch in range(NCH):
                    for e in range(2):
                        if ch >= 2:
                            pe.wait_ge(gram_copied[e], NCH * t + ch - 1)
                    for m in range(CH // GS):
                        b = CH * ch + GS * m
                        o = (m % BG) * GS * NC
                        last = nc.tensor.matmul(
                            gram[:, ch % 2, m // BG, o:o + GS * NC],
                            vecsT[:, s, b:b + GS, :].rearrange("d b v -> d (b v)"),
                            vecsT[:, s, b:b + GS, 0:NC], start=True, stop=True)
                        if ch == 0 and m == 0:
                            last.then_inc(tile_transposed, 1)
                    last.then_inc(gram_full, 1)

                pe.wait_ge(gram_copied[0], NCH * (t + 1))
                pe.wait_ge(gram_copied[1], NCH * (t + 1))
                if s == 0:
                    pe.wait_ge(wz_loaded, 16 * NC)
                    pe.wait_ge(wd_ready, 1)
                    pe.wait_ge(w2_loaded, 16)
                pe.wait_ge(mlp_free, t + 1)
                for n in range(N1T):
                    acc = mlp[:, n // 2, (n % 2) * P:(n % 2 + 1) * P]
                    nc.tensor.matmul(acc, Wd[:, n * P:(n + 1) * P], denseT[:, s, :], start=True, stop=False)
                    for c in range(SLOTS):
                        last = nc.tensor.matmul(acc, Wz[:, c, n * P:(n + 1) * P], Z[:, c, :],
                                                start=False, stop=(c == SLOTS - 1))
                    if n % 2:
                        last.then_inc(l1_full[n // 2], 1)
                pe.wait_ge(h1_ready[0], t + 1)
                pe.wait_ge(h1_ready[1], t + 1)
                for e in range(N2T):
                    for n in range(N1T):
                        last = nc.tensor.matmul(mlp[:, e, 0:P], W2s[:, n, e * P:(e + 1) * P], h1[:, n, :],
                                                start=(n == 0), stop=(n == N1T - 1))
                    last.then_inc(l2_full[e], 1)
                pe.wait_ge(h2_ready[0], t + 1)
                pe.wait_ge(h2_ready[1], t + 1)
                for e in range(N2T):
                    last = nc.tensor.matmul(mlp[0:1, 0, 0:P], cols[:, N1T + N2T + e:N1T + N2T + e + 1],
                                            h2[:, e, :], start=(e == 0), stop=(e == N2T - 1))
                last.then_inc(l3_full, 1)

            with pe.Fori(0, NT // 2) as i:
                for s in range(2):
                    tile(i, s)


_TABLES = [f'tbl_{f}' for f in range(26)]
_INS = ['r_dense_features', 'ids'] + _TABLES + ['W_top1', 'b_top1', 'W_top2', 'b_top2', 'W_top3']


def kernel(**inputs):
    import numpy as np
    import concourse.bacc as bacc
    from concourse.bass_utils import run_bass_kernel_spmd

    nc = bacc.Bacc("TRN2", target_bir_lowering=False, num_devices=1)
    arrays, aps = {}, {}
    for name in _INS:
        a = np.ascontiguousarray(inputs[name])
        arrays[f"in_{name}_dram"] = a
        aps[name] = nc.dram_tensor(f"in_{name}_dram", a.shape, mybir.dt.from_np(a.dtype), kind="ExternalInput").ap()
    out = nc.dram_tensor("out_0_dram", (aps['ids'].shape[0], 1), F32, kind="ExternalOutput").ap()
    dlrm_tower_kernel(nc, aps['r_dense_features'], aps['ids'], [aps[t] for t in _TABLES], aps['W_top1'],
                      aps['b_top1'], aps['W_top2'], aps['b_top2'], aps['W_top3'], out)
    r = run_bass_kernel_spmd(nc, [arrays], core_ids=[0])
    return r.results[0]["out_0_dram"]
```

```python
from contextlib import ExitStack, nullcontext

import concourse.bass as bass
from concourse import mybir

ALU = mybir.AluOpType
ACT = mybir.ActivationFunctionType
F32 = mybir.dt.float32
U32 = mybir.dt.uint32
F32R = mybir.dt.float32r

P = 128
QUAD = 32


def dlrm_tower_kernel(nc, dense, ids, tables, W1, b1, W2, b2, W3, out):
    B, D = dense.shape
    F = ids.shape[1]
    NV = F + 1
    NT = B // P
    N1 = W1.shape[1]
    N2 = W2.shape[1]
    N1T, N2T = N1 // P, N2 // P
    NC = NV - 1
    ZC = -(-NC // 4)
    COL0 = [min(k * ZC, NC - ZC) for k in range(4)]
    GS = 4
    CH = 32
    NCH = P // CH
    BG = CH // GS // 2

    NPK = 4
    small = min(tb.shape[0] for tb in tables)
    picks = [v for v in range(1, NV) if tables[v - 1].shape[0] == small][-NPK:]
    R = 8
    R_ACT = 2
    R_DVE = R - R_ACT
    LO_AT = 2
    KP = small // R
    assert KP * R == small and KP <= P and B <= 512 and len(picks) == NPK

    TPG = 4
    gathered_vs = [v for v in range(NV) if v not in picks]
    GROUPS = [gathered_vs[n:n + TPG] for n in range(0, len(gathered_vs), TPG)]
    NG = len(GROUPS)
    GPE = NG // 2
    assert D == P and B % (2 * P) == 0 and N1T == 4 and N2T == 2 and NG % 2 == 0

    def runs(vs):
        out, n = [], 0
        while n < len(vs):
            m = n + 1
            while m < len(vs) and vs[m] == vs[m - 1] + 1:
                m += 1
            out.append((n, vs[n], m - n))
            n = m
        return out

    dense_t = dense.rearrange("(p t) d -> p t d", t=NT)
    ids_t = ids.bitcast(U32).rearrange("(p t) f -> p t f", t=NT)

    with ExitStack() as ctx:
        def sb(name, shape, dt=F32):
            return ctx.enter_context(nc.sbuf_tensor(name, shape, dt))

        def psum(name, shape):
            return ctx.enter_context(nc.psum_tensor(name, shape, F32))

        def sem(name):
            return ctx.enter_context(nc.semaphore(name))

        def two(name):
            return [sem(name + "0"), sem(name + "1")]

        ident = sb("ident", [P, P])
        idx = sb("idx", [P, 2, F], U32)
        vecs = sb("vecs", [P, 2, NV, D])
        vecsT = sb("vecsT", [P, 2, P, QUAD])
        denseT = sb("denseT", [P, 2, P])
        Z = sb("Z", [P, ZC, P])
        Wz = sb("Wz", [P, ZC, N1])
        Wda = sb("Wda", [P, N1])
        Wdb = sb("Wdb", [P, N1])
        Wd = sb("Wd", [P, N1])
        W2s = sb("W2s", [P, N1T, N2])
        NR = N1T + 2 * N2T
        rows = sb("rows", [NR, P])
        cols = sb("cols", [P, NR])
        h1 = sb("h1", [P, N1T, P])
        h2 = sb("h2", [P, N2T, P])
        y = sb("y", [1, P, NT])
        zeros = sb("zeros", [P, N1])
        ids_all = sb("ids_all", [P, NT, F], U32)
        idsf = sb("idsf", [P, NT, F])
        row_no = sb("row_no", [P, R])
        row_neg = sb("row_neg", [P, R])
        wanted = sb("wanted", [KP, NPK, B])
        apart = sb("apart", [KP, R_ACT, B])
        table = sb("table", [KP, NPK, R, D])
        onehot = sb("onehot", [KP, 2, R, B], F32R)
        tab_hi = sb("tab_hi", [KP, NPK, R, D], F32R)
        tab_lo = sb("tab_lo", [KP, NPK, R, D], F32R)
        picked = sb("picked", [P, NPK, B])

        tpb = psum("tpb", [P, 2, TPG * P])
        gram = psum("gram", [P, 2, 2, 512])
        mlp = psum("mlp", [P, 2, 512])
        l2_acc = [mlp[:, 0, 0:P], gram[:, 0, 0, 0:P]]
        l3_acc = mlp[0:1, 1, 0:P]

        idx_loaded = two("idx_loaded")
        dense_loaded = two("dense_loaded")
        gathered = [[sem(f"gathered{s}_{g}") for g in range(NG)] for s in range(2)]
        ids_all_loaded = sem("ids_all_loaded")
        idsf_ready = sem("idsf_ready")
        row_no_ready = sem("row_no_ready")
        table_loaded = [sem(f"table_loaded{u}") for u in range(NPK)]
        hi_ready = sem("hi_ready")
        lo_ready = sem("lo_ready")
        ids_spread = sem("ids_spread")
        wanted_ready = sem("wanted_ready")
        apart_ready = sem("apart_ready")
        onehot_dve = sem("onehot_dve")
        onehot_act = sem("onehot_act")
        selected = sem("selected")
        picked_ready = sem("picked_ready")
        ident_zero = sem("ident_zero")
        ident_ready = sem("ident_ready")
        zeros_ready = sem("zeros_ready")
        wz_zeroed = sem("wz_zeroed")
        pad_zeroed = sem("pad_zeroed")
        wz_loaded = sem("wz_loaded")
        wd_loaded = sem("wd_loaded")
        wd_ready = sem("wd_ready")
        w2_loaded = sem("w2_loaded")
        rows_loaded = sem("rows_loaded")
        cols_full = sem("cols_full")
        cols_ready = sem("cols_ready")
        tile_transposed = sem("tile_transposed")
        tp_full = two("tp_full")
        tp_copied = two("tp_copied")
        gram_full = sem("gram_full")
        gram_copied = two("gram_copied")
        l1_full = two("l1_full")
        h1_ready = two("h1_ready")
        l2_full = two("l2_full")
        h2_ready = two("h2_ready")
        l3_full = sem("l3_full")
        y_copied = sem("y_copied")
        y_stored = sem("y_stored")

        block = ctx.enter_context(nc.Block())

        SETUP_GROUPS = [[], [0], [1, 2], [3], [4, 5]]

        def if_next(eng, i, s):
            return eng.If(i < NT // 2 - 1) if s else nullcontext()

        def after(i, s):
            return (i + 1, 0) if s else (i, 1)

        @block.sync
        def _(sp):
            def load_tile(t, s):
                sp.dma_start(idx[:, s, :], ids_t[:, t, :]).then_inc(idx_loaded[s], 16)
                sp.dma_start(vecs[:, s, 0, :], dense_t[:, t, :]).then_inc(dense_loaded[s], 16)

            sp.dma_start(ids_all[:], ids_t).then_inc(ids_all_loaded, 16)
            load_tile(0, 0)
            sp.dma_start(rows[0:N1T, :], b1.rearrange("(n p) -> n p", p=P)).then_inc(rows_loaded, 16)
            sp.dma_start(rows[N1T:N1T + N2T, :], b2.rearrange("(n p) -> n p", p=P)).then_inc(rows_loaded, 16)
            sp.dma_start(rows[N1T + N2T:NR, :], W3.rearrange("(n p) o -> n (p o)", p=P)).then_inc(rows_loaded, 16)
            for u, v in enumerate(picks):
                sp.dma_start(table[:, u], tables[v - 1].rearrange("(p r) d -> p r d", r=R)
                             ).then_inc(table_loaded[u], 16)
            load_tile(1, 1)
            sp.dma_start(Wda[:], W1[0:D, :]).then_inc(wd_loaded, 16)
            sp.dma_start(Wdb[:], W1[W1.shape[0] - D:W1.shape[0], :]).then_inc(wd_loaded, 16)
            sp.wait_ge(wz_zeroed, 1)
            row = D
            for c in range(NC):
                k = min(c // ZC, 3)
                p0, n = QUAD * k + c + 1, NC - c
                sp.dma_start(Wz[p0:p0 + n, c - COL0[k], :], W1[row:row + n, :]).then_inc(wz_loaded, 16)
                row += n
            sp.dma_start(W2s[:], W2.rearrange("(k p) n -> p k n", p=P)).then_inc(w2_loaded, 16)
            with sp.Fori(1, NT // 2) as i:
                for s in range(2):
                    sp.wait_ge(tile_transposed, 2 * i + s - 1)
                    load_tile(2 * i + s, s)
            sp.wait_ge(y_copied, NT)
            sp.dma_start(out.rearrange("b o -> o b"), y[:].rearrange("o p t -> o (p t)")).then_inc(y_stored, 16)
            sp.wait_ge(y_stored, 16)

        @block.gpsimd
        def _(pool):
            nc.gpsimd.memset(ident[:], 0.0).then_inc(ident_zero, 1)
            nc.gpsimd.iota(row_no[:], [[1, R]], base=0, channel_multiplier=R,
                           allow_small_or_imprecise_dtypes=True).then_inc(row_no_ready, 1)
            nc.gpsimd.iota(row_neg[:], [[-1, R]], base=0, channel_multiplier=-R,
                           allow_small_or_imprecise_dtypes=True).then_inc(row_no_ready, 1)
            pool.wait_ge(ident_zero, 1)
            nc.gpsimd.affine_select(out=ident[:], in_=ident[:], compare_op=ALU.not_equal, fill=1.0, base=0,
                                    pattern=[[-1, P]], channel_multiplier=1).then_inc(ident_ready, 1)

            def gather(s):
                for g, vs in enumerate(GROUPS):
                    for v in vs:
                        if v:
                            nc.gpsimd.indirect_dma_start(
                                vecs[:, s, v, :], None, tables[v - 1],
                                bass.IndirectOffsetOnAxis(idx[:, s, v - 1:v], 0)).then_inc(gathered[s][g], 16)

            for s in range(2):
                pool.wait_ge(idx_loaded[s], 16)
                gather(s)
            with pool.Fori(1, NT // 2) as i:
                for s in range(2):
                    pool.wait_ge(tile_transposed, 2 * i + s - 1)
                    pool.wait_ge(idx_loaded[s], 16 * (i + 1))
                    gather(s)

        def copy_out(e, eng, copy, relu):

            def transposes(i, s, groups):
                for g in groups:
                    if g % 2 != e:
                        continue
                    eng.wait_ge(tp_full[e], GPE * (2 * i + s) + g // 2 + 1)
                    if g == 0:
                        copy(denseT[:, s, :], tpb[:, e, 0:P])
                    for n, v0, nv in runs(GROUPS[g]):
                        last = copy(vecsT[:, s, :, v0:v0 + nv],
                                    tpb[:, e, n * P:(n + nv) * P].rearrange("d (v b) -> d b v", v=nv))
                    last.then_inc(tp_copied[e], 1)

            def products(i, s):
                for ch in range(NCH):
                    eng.wait_ge(gram_full, NCH * (2 * i + s) + ch + 1)
                    for j in (2 * e, 2 * e + 1):
                        for k in range(4):
                            src = gram[QUAD * j:QUAD * (j + 1), ch % 2, :, 0:BG * GS * NC].rearrange(
                                "r a (q j c) -> r j a q c", q=BG, j=GS)[:, j, :, :, COL0[k]:COL0[k] + ZC]
                            dst = Z[QUAD * k:QUAD * (k + 1), :, CH * ch:CH * (ch + 1)].rearrange(
                                "r c (a q j) -> r j a q c", q=BG, j=GS)[:, j]
                            last = copy(dst, src)
                    last.then_inc(gram_copied[e], 1)

            def layer1(i, s):
                eng.wait_ge(l1_full[e], 2 * i + s + 1)
                for n in (2 * e, 2 * e + 1):
                    last = relu(h1[:, n, :], mlp[:, e, (n % 2) * P:(n % 2 + 1) * P], cols[:, n:n + 1])
                last.then_inc(h1_ready[e], 1)

            def layer2(i, s):
                eng.wait_ge(l2_full[e], 2 * i + s + 1)
                relu(h2[:, e, :], l2_acc[e], cols[:, N1T + e:N1T + e + 1]).then_inc(h2_ready[e], 1)

            return transposes, products, layer1, layer2

        @block.vector
        def _(dve):
            def relu(dst, src, bias):
                return nc.vector.tensor_scalar(dst, src, bias, 0.0, ALU.add, ALU.max)

            transposes, products, layer1, layer2 = copy_out(0, dve, nc.vector.tensor_copy, relu)

            nc.vector.memset(zeros[:], 0.0).then_inc(zeros_ready, 1)
            dve.wait_ge(ids_all_loaded, 16)
            nc.vector.tensor_copy(idsf[:], ids_all[:]).then_inc(idsf_ready, 1)
            dve.wait_ge(cols_full, 1)
            nc.vector.tensor_copy(cols[:], mlp[:, 0, 0:NR]).then_inc(cols_ready, 1)
            dve.wait_ge(row_no_ready, 2)
            for u in range(NPK):
                dve.wait_ge(wanted_ready, u + 1)
                if u >= 2:
                    dve.wait_ge(selected, u - 1)
                for r in range(R_DVE):
                    nc.vector.tensor_scalar(onehot[:, u % 2, r, :], gram[0:KP, u // 2, u % 2, :], row_no[0:KP, r:r + 1],
                                            None, ALU.is_equal).then_inc(onehot_dve, 1)
                    if r == LO_AT:
                        dve.wait_ge(hi_ready, u + 1)
                        nc.vector.tensor_tensor(tab_lo[:, u], table[:, u], tab_hi[:, u].bitcast(F32),
                                                ALU.subtract).then_inc(lo_ready, 1)
                if u >= 2:
                    transposes(0, 0, SETUP_GROUPS[u - 1])
            transposes(0, 0, SETUP_GROUPS[NPK - 1])
            dve.wait_ge(wd_loaded, 32)
            nc.vector.tensor_tensor(Wd[:], Wda[:], Wdb[:], ALU.add).then_inc(wd_ready, 1)
            dve.wait_ge(cols_ready, 1)
            transposes(0, 0, SETUP_GROUPS[NPK])

            with dve.Fori(0, NT // 2) as i:
                for s in range(2):
                    products(i, s)
                    with if_next(dve, i, s):
                        transposes(*after(i, s), [0])
                    layer1(i, s)
                    layer2(i, s)
                    with if_next(dve, i, s):
                        transposes(*after(i, s), [1])
                    dve.wait_ge(l3_full, 2 * i + s + 1)
                    nc.vector.tensor_copy(y[:, :, bass.ds(2 * i + s, 1)].rearrange("o p t -> o (p t)"),
                                          l3_acc).then_inc(y_copied, 1)
                    with if_next(dve, i, s):
                        transposes(*after(i, s), range(2, NG))

        @block.scalar
        def _(act):
            def relu(dst, src, bias):
                return nc.scalar.activation(dst, src, ACT.Relu, bias=bias)

            transposes, products, layer1, layer2 = copy_out(1, act, nc.scalar.copy, relu)

            def place_picked(i, s):
                first = (2 * i + s) * P if isinstance(i, int) else nc.s_assert_within((2 * i + s) * P, 0, B - P)
                for u, v in enumerate(picks):
                    nc.scalar.copy(vecsT[:, s, :, v], picked[:, u, bass.ds(first, P)])

            act.wait_ge(zeros_ready, 1)
            for s in range(2):
                last = nc.scalar.copy(vecsT[:, s, 0:P // 2, NV:QUAD],
                                      zeros[:, 0:P // 2 * (QUAD - NV)].rearrange("p (b v) -> p b v", v=QUAD - NV))
                last = nc.scalar.copy(vecsT[:, s, P // 2:P, NV:QUAD],
                                      zeros[:, 0:P // 2 * (QUAD - NV)].rearrange("p (b v) -> p b v", v=QUAD - NV))
            last.then_inc(pad_zeroed, 1)
            act.wait_ge(row_no_ready, 2)

            def spread(u):
                act.wait_ge(ids_spread, u + 1)
                nc.scalar.copy(wanted[:, u, :], gram[0:KP, u // 2, u % 2, :]).then_inc(wanted_ready, 1)

            def high_part(u):
                act.wait_ge(table_loaded[u], 16)
                nc.scalar.copy(tab_hi[:, u], table[:, u]).then_inc(hi_ready, 1)

            def one_hot(u):
                if u >= 2:
                    act.wait_ge(selected, u - 1)
                if u >= 1:
                    act.wait_ge(onehot_act, R_ACT * u)
                act.wait_ge(wanted_ready, u + 1)
                for r in range(R_ACT):
                    nc.scalar.activation(apart[:, r, :], wanted[:, u, :], ACT.Abs,
                                         bias=row_neg[0:KP, R_DVE + r:R_DVE + r + 1]).then_inc(apart_ready, 1)
                for r in range(R_ACT):
                    act.wait_ge(apart_ready, R_ACT * u + r + 1)
                    nc.scalar.activation(onehot[:, u % 2, R_DVE + r, :], apart[:, r, :], ACT.Relu,
                                         bias=1.0, scale=-1.0).then_inc(onehot_act, 1)

            def keep_picked(u):
                act.wait_ge(selected, u + 1)
                nc.scalar.copy(picked[:, u, :], mlp[:, u % 2, :]).then_inc(picked_ready, 1)

            spread(0)
            high_part(0)
            for u in range(1, NPK):
                spread(u)
            one_hot(0)
            high_part(1)
            one_hot(1)
            for g in range(ZC):
                last = nc.scalar.copy(Wz[:, g, :], zeros[:])
            last.then_inc(wz_zeroed, 1)
            high_part(2)
            keep_picked(0)
            one_hot(2)
            high_part(3)
            keep_picked(1)
            one_hot(3)
            transposes(0, 0, [1])
            keep_picked(2)
            keep_picked(3)
            transposes(0, 0, [3])
            act.wait_ge(cols_ready, 1)
            act.wait_ge(picked_ready, NPK)
            place_picked(0, 0)
            transposes(0, 0, [5])

            with act.Fori(0, NT // 2) as i:
                for s in range(2):
                    products(i, s)
                    with if_next(act, i, s):
                        place_picked(*after(i, s))
                        transposes(*after(i, s), [0])
                    layer1(i, s)
                    layer2(i, s)
                    with if_next(act, i, s):
                        transposes(*after(i, s), range(1, NG))

        @block.tensor
        def _(pe):
            def transposes(i, s, groups):
                t = 2 * i + s
                for g in groups:
                    e = g % 2
                    if isinstance(i, int) and GPE * t + g // 2 == 0:
                        pass
                    else:
                        pe.wait_ge(tp_copied[e], GPE * t + g // 2)
                    if g == 0:
                        pe.wait_ge(dense_loaded[s], 16 * (i + 1))
                    pe.wait_ge(gathered[s][g], 16 * (len(GROUPS[g]) - (g == 0)) * (i + 1))
                    for n, v in enumerate(GROUPS[g]):
                        last = nc.tensor.transpose(tpb[:, e, n * P:(n + 1) * P], vecs[:, s, v, :], ident[:])
                    last.then_inc(tp_full[e], 1)

            def dense_layer1(s):
                for n in range(N1T):
                    nc.tensor.matmul(mlp[:, n // 2, (n % 2) * P:(n % 2 + 1) * P], Wd[:, n * P:(n + 1) * P],
                                     denseT[:, s, :], start=(n % 2 == 0), stop=False, skip_group_check=True)

            def products(i, s):
                t = 2 * i + s
                for e in range(2):
                    pe.wait_ge(tp_copied[e], GPE * (t + 1))
                for ch in range(NCH):
                    if ch >= 2:
                        for e in range(2):
                            pe.wait_ge(gram_copied[e], NCH * t + ch - 1)
                    for m in range(CH // GS):
                        b = CH * ch + GS * m
                        o = (m % BG) * GS * NC
                        last = nc.tensor.matmul(
                            gram[:, ch % 2, m // BG, o:o + GS * NC],
                            vecsT[:, s, b:b + GS, :].rearrange("d b v -> d (b v)"),
                            vecsT[:, s, b:b + GS, 0:NC], start=True, stop=True)
                        if ch == 0 and m == 0:
                            last.then_inc(tile_transposed, 1)
                    last.then_inc(gram_full, 1)

            def layers12(i, s):
                t = 2 * i + s
                for e in range(2):
                    pe.wait_ge(gram_copied[e], NCH * (t + 1))
                pe.wait_ge(wz_loaded, 16 * NC)
                for n in range(N1T):
                    for g in range(ZC):
                        last = nc.tensor.matmul(mlp[:, n // 2, (n % 2) * P:(n % 2 + 1) * P],
                                                Wz[:, g, n * P:(n + 1) * P], Z[:, g, :], start=False,
                                                stop=(g == ZC - 1), skip_group_check=True)
                    if n % 2:
                        last.then_inc(l1_full[n // 2], 1)
                pe.wait_ge(w2_loaded, 16)
                for half in range(2):
                    pe.wait_ge(h1_ready[half], t + 1)
                    for e in range(N2T):
                        for n in (2 * half, 2 * half + 1):
                            last = nc.tensor.matmul(l2_acc[e], W2s[:, n, e * P:(e + 1) * P], h1[:, n, :],
                                                    start=(n == 0), stop=(n == N1T - 1))
                        if half:
                            last.then_inc(l2_full[e], 1)

            def layer3(i, s):
                for e in range(N2T):
                    pe.wait_ge(h2_ready[e], 2 * i + s + 1)
                    last = nc.tensor.matmul(l3_acc, cols[:, N1T + N2T + e:N1T + N2T + e + 1],
                                            h2[:, e, :], start=(e == 0), stop=(e == N2T - 1))
                last.then_inc(l3_full, 1)

            pe.wait_ge(ident_ready, 1)
            pe.wait_ge(idsf_ready, 1)
            for u, v in enumerate(picks):
                for t in range(NT):
                    last = nc.tensor.matmul(gram[:, u // 2, u % 2, t * P:(t + 1) * P],
                                            idsf[:, t, v - 1:v].to_broadcast([P, P]), ident[:],
                                            start=True, stop=True)
                last.then_inc(ids_spread, 1)
                if u == 0:
                    pe.wait_ge(rows_loaded, 48)
                    nc.tensor.transpose(mlp[:, 0, 0:NR], rows[:], ident[0:NR, 0:NR]).then_inc(cols_full, 1)
            pe.wait_ge(cols_ready, 1)
            for u in range(NPK):
                if u >= 2:
                    pe.wait_ge(picked_ready, u - 1)
                pe.wait_ge(hi_ready, u + 1)
                for r in range(R):
                    if r < R_DVE:
                        pe.wait_ge(onehot_dve, R_DVE * u + r + 1)
                    else:
                        pe.wait_ge(onehot_act, R_ACT * u + r - R_DVE + 1)
                    nc.tensor.matmul(mlp[:, u % 2, :], tab_hi[:, u, r, :], onehot[:, u % 2, r, :],
                                     start=(r == 0), stop=False)
                    if r == LO_AT:
                        pe.wait_ge(lo_ready, u + 1)
                    for q in range(LO_AT + 1) if r == LO_AT else [r] if r > LO_AT else []:
                        last = nc.tensor.matmul(mlp[:, u % 2, :], tab_lo[:, u, q, :], onehot[:, u % 2, q, :],
                                                start=False, stop=(q == R - 1))
                last.then_inc(selected, 1)
                transposes(0, 0, SETUP_GROUPS[u])
            transposes(0, 0, SETUP_GROUPS[NPK])
            pe.wait_ge(picked_ready, NPK)
            pe.wait_ge(wd_ready, 1)
            dense_layer1(0)
            pe.wait_ge(pad_zeroed, 1)
            pe.wait_ge(onehot_dve, R_DVE * NPK)

            with pe.Fori(0, NT // 2) as i:
                for s in range(2):
                    products(i, s)
                    with if_next(pe, i, s):
                        transposes(*after(i, s), [0])
                    layers12(i, s)
                    with if_next(pe, i, s):
                        transposes(*after(i, s), [1])
                    layer3(i, s)
                    with if_next(pe, i, s):
                        transposes(*after(i, s), range(2, NG - 1))
                        pe.wait_ge(y_copied, 2 * i + s + 1)
                        dense_layer1(1 - s)
                        transposes(*after(i, s), [NG - 1])


_TABLES = [f'tbl_{f}' for f in range(26)]
_INS = ['r_dense_features', 'ids'] + _TABLES + ['W_top1', 'b_top1', 'W_top2', 'b_top2', 'W_top3']


def kernel(**inputs):
    import numpy as np
    import concourse.bacc as bacc
    from concourse.bass_utils import run_bass_kernel_spmd

    nc = bacc.Bacc("TRN2", target_bir_lowering=False, num_devices=1)
    arrays, aps = {}, {}
    for name in _INS:
        a = np.ascontiguousarray(inputs[name])
        arrays[f"in_{name}_dram"] = a
        aps[name] = nc.dram_tensor(f"in_{name}_dram", a.shape, mybir.dt.from_np(a.dtype), kind="ExternalInput").ap()
    out = nc.dram_tensor("out_0_dram", (aps['ids'].shape[0], 1), F32, kind="ExternalOutput").ap()
    dlrm_tower_kernel(nc, aps['r_dense_features'], aps['ids'], [aps[t] for t in _TABLES], aps['W_top1'],
                      aps['b_top1'], aps['W_top2'], aps['b_top2'], aps['W_top3'], out)
    r = run_bass_kernel_spmd(nc, [arrays], core_ids=[0])
    return r.results[0]["out_0_dram"]
```

```python
from contextlib import ExitStack, nullcontext

import concourse.bass as bass
from concourse import mybir

ALU = mybir.AluOpType
ACT = mybir.ActivationFunctionType
F32 = mybir.dt.float32
U32 = mybir.dt.uint32
F32R = mybir.dt.float32r

P = 128
QUAD = 32


def dlrm_tower_kernel(nc, dense, ids, tables, W1, b1, W2, b2, W3, out):
    B, D = dense.shape
    F = ids.shape[1]
    NV = F + 1
    NT = B // P
    N1 = W1.shape[1]
    N2 = W2.shape[1]
    N1T, N2T = N1 // P, N2 // P
    ZC = 4
    DUP, ND = 4, 3
    ROWS = list(range(NV)) + list(range(DUP, DUP + ND))
    QUADS = [(10, 1, 23), (15, 11, 0), (19, 15, 6), (10, 7, 19)]
    GS = 4
    CH = 32
    NCH = P // CH
    BG = CH // GS // 2

    NPK = 7
    small = min(tb.shape[0] for tb in tables)
    picks = [v for v in range(1, NV) if tables[v - 1].shape[0] == small][-NPK:]
    R = 8
    ON_ACT = [1, 2, 2, 2, 1, 2, 1]
    KP = small // R
    assert KP * R == small and small <= 2048 and KP <= P and B <= 512 and len(picks) == NPK == len(ON_ACT)

    TPG = 4
    gathered_vs = [v for v in range(NV) if v not in picks]
    FULL = (len(gathered_vs) - 1) // TPG * TPG
    GROUPS = [gathered_vs[n:n + TPG] for n in range(0, FULL, TPG)] + [gathered_vs[FULL:-1], gathered_vs[-1:]]
    NG = len(GROUPS)
    GPE = NG // 2
    assert D == P and B % (2 * P) == 0 and N1T == 4 and N2T == 2 and NG == 6
    assert NCH == 4 and len(ROWS) <= QUAD and BG * GS * NV <= 512

    def runs(vs):
        out, n = [], 0
        while n < len(vs):
            m = n + 1
            while m < len(vs) and vs[m] == vs[m - 1] + 1:
                m += 1
            out.append((n, vs[n], m - n))
            n = m
        return out

    dense_t = dense.rearrange("(p t) d -> p t d", t=NT)
    ids_t = ids.bitcast(U32).rearrange("(p t) f -> p t f", t=NT)

    with ExitStack() as ctx:
        def sb(name, shape, dt=F32):
            return ctx.enter_context(nc.sbuf_tensor(name, shape, dt))

        def psum(name, shape):
            return ctx.enter_context(nc.psum_tensor(name, shape, F32))

        def sem(name):
            return ctx.enter_context(nc.semaphore(name))

        def two(name):
            return [sem(name + "0"), sem(name + "1")]

        ident = sb("ident", [P, P])
        idx = sb("idx", [P, 2, F], U32)
        vecs = sb("vecs", [P, 2, NV, D])
        vecsT = sb("vecsT", [P, 2, P, QUAD])
        denseT = sb("denseT", [P, 2, P])
        Z = sb("Z", [P, ZC, P])
        Wz = sb("Wz", [P, ZC, N1])
        Wda = sb("Wda", [P, N1])
        Wdb = sb("Wdb", [P, N1])
        Wd = sb("Wd", [P, N1])
        W2s = sb("W2s", [P, N1T, N2])
        NR = N1T + 2 * N2T
        rows = sb("rows", [NR, P])
        cols = sb("cols", [P, NR])
        h1 = sb("h1", [P, N1T, P])
        h2 = sb("h2", [P, N2T, P])
        y = sb("y", [1, P, NT])
        zeros = sb("zeros", [P, N1])
        ids_all = sb("ids_all", [P, NT, F], U32)
        idsf = sb("idsf", [P, NT, F])
        idsT = sb("idsT", [F, B], F32R)
        ident_r = sb("ident_r", [F, F], F32R)
        row_no = sb("row_no", [P, R])
        row_neg = sb("row_neg", [P, R])
        wanted = sb("wanted", [KP, NPK, B])
        table = sb("table", [KP, NPK, R, D])
        onehot = sb("onehot", [KP, 2, R, B], F32R)
        tab_hi = sb("tab_hi", [KP, 3, R, D], F32R)
        tab_lo = sb("tab_lo", [KP, 2, R, D], F32R)
        picked = sb("picked", [P, NPK, B])

        gram = psum("gram", [P, 3, 2, 512])
        mlp = psum("mlp", [P, 2, 512])
        BUFFER = [0, 1, 2, 0]
        tp_bank = [gram[:, n // 2, n % 2, :] for n in (2, 3, 4, 5, 0, 1)]
        l2_acc = [gram[:, 2, 0, 0:P], gram[:, 1, 0, 0:P]]
        spread_ids = [gram[:, n // 2 % 3, n % 2, :] for n in range(NPK)]
        l3_acc = gram[0:1, 2, 1, 0:P]

        idx_loaded = two("idx_loaded")
        dense_loaded = two("dense_loaded")
        gathered = [[sem(f"gathered{s}_{g}") for g in range(NG)] for s in range(2)]
        ids_all_loaded = sem("ids_all_loaded")
        idsf_ready = sem("idsf_ready")
        idsT_full = sem("idsT_full")
        idsT_ready = sem("idsT_ready")
        row_no_ready = sem("row_no_ready")
        table_loaded = [sem(f"table_loaded{u}") for u in range(NPK)]
        hi_ready = sem("hi_ready")
        lo_ready = sem("lo_ready")
        ids_spread = sem("ids_spread")
        wanted_ready = sem("wanted_ready")
        apart_ready = sem("apart_ready")
        onehot_dve = sem("onehot_dve")
        onehot_act = sem("onehot_act")
        selected = sem("selected")
        picked_ready = sem("picked_ready")
        last_placed = sem("last_placed")
        ident_zero = sem("ident_zero")
        ident_ready = sem("ident_ready")
        zeros_ready = sem("zeros_ready")
        wz_zeroed = sem("wz_zeroed")
        pad_zeroed = sem("pad_zeroed")
        wz_loaded = sem("wz_loaded")
        wd_loaded = sem("wd_loaded")
        wd_ready = sem("wd_ready")
        w2_loaded = sem("w2_loaded")
        rows_loaded = sem("rows_loaded")
        cols_full = sem("cols_full")
        cols_ready = sem("cols_ready")
        tile_transposed = sem("tile_transposed")
        tp_full = two("tp_full")
        tp_copied = two("tp_copied")
        gram_full = sem("gram_full")
        lower_filled = two("lower_filled")
        gram_copied = two("gram_copied")
        l1_full = two("l1_full")
        h1_ready = two("h1_ready")
        l2_full = two("l2_full")
        h2_ready = two("h2_ready")
        l3_full = sem("l3_full")
        y_copied = sem("y_copied")
        y_stored = sem("y_stored")

        block = ctx.enter_context(nc.Block())

        def made(u, on_act):
            return sum(n if on_act else R - n for n in ON_ACT[:u])

        SETUP_GROUPS = [[], [], [0, 1], [2], [3], [4, 5], []]
        assert len(SETUP_GROUPS) == NPK and NPK <= 8

        def wz_parts():
            def column(k, p, g):
                rows, upper, lower = QUADS[k]
                return (upper if p < rows else lower) + g

            def run(x, y, k, p, g, dp, dg):
                n = 0
                while (y + n < NV and p < len(ROWS) and g < ZC
                       and (column(k, p, g), ROWS[p]) == ((x, y + n) if dp else (y + n, x))):
                    n, p, g = n + 1, p + dp, g + dg
                return n

            found = {}
            for x in range(NV - 1):
                y = x + 1
                while y < NV:
                    n, *place = max((run(x, y, k, p, g, dp, 1 - dp), k, p, g, dp) for k in range(4)
                                    for p in range(len(ROWS)) for g in range(ZC) for dp in (0, 1))
                    assert n, "a pair has no place"
                    found[x, y] = n, place
                    y += n

            parts, done = [], set()
            for (x, y), (n, (k, p, g, dp)) in found.items():
                if (x, y) in done:
                    continue
                row = D + x * (NV - 1) - x * (x - 1) // 2 + y - x - 1
                p0 = QUAD * k + p
                if dp:
                    parts.append((Wz[p0:p0 + n, g, :], W1[row:row + n, :]))
                elif found.get((x + 1, y)) == (n, [k, p + 1, g, 0]):
                    done.add((x + 1, y))
                    apart = NV - 2 - x
                    parts.append((Wz[p0:p0 + 2, g:g + n, :],
                                  W1[row:row + 2 * apart, :].rearrange("(o g) n -> o g n", o=2)[:, 0:n, :]))
                else:
                    parts.append((Wz[p0:p0 + 1, g:g + n, :],
                                  W1[row:row + n, :].rearrange("(o g) n -> o g n", o=1)))
            return parts

        def if_next(eng, i, s):
            return eng.If(i < NT // 2 - 1) if s else nullcontext()

        def if_prev(eng, i, s):
            return nullcontext() if s else eng.If(i > 0)

        def after(i, s):
            return (i + 1, 0) if s else (i, 1)

        @block.sync
        def _(sp):
            def load_dense(t, s):
                sp.dma_start(vecs[:, s, 0, :], dense_t[:, t, :]).then_inc(dense_loaded[s], 16)

            def load_table(u):
                sp.dma_start(table[:, u], tables[picks[u] - 1].rearrange("(p r) d -> p r d", r=R)
                             ).then_inc(table_loaded[u], 16)

            sp.dma_start(ids_all[:], ids_t).then_inc(ids_all_loaded, 16)
            load_table(0)
            load_table(1)
            load_dense(0, 0)
            sp.dma_start(rows[0:N1T, :], b1.rearrange("(n p) -> n p", p=P)).then_inc(rows_loaded, 16)
            sp.dma_start(rows[N1T:N1T + N2T, :], b2.rearrange("(n p) -> n p", p=P)).then_inc(rows_loaded, 16)
            sp.dma_start(rows[N1T + N2T:NR, :], W3.rearrange("(n p) o -> n (p o)", p=P)).then_inc(rows_loaded, 16)
            for u in range(2, NPK):
                load_table(u)
            load_dense(1, 1)
            sp.dma_start(Wda[:], W1[0:D, :]).then_inc(wd_loaded, 16)
            sp.dma_start(Wdb[:], W1[W1.shape[0] - D:W1.shape[0], :]).then_inc(wd_loaded, 16)
            sp.wait_ge(wz_zeroed, 1)
            for dst, src in wz_parts():
                sp.dma_start(dst, src).then_inc(wz_loaded, 16)
            sp.dma_start(W2s[:], W2.rearrange("(k p) n -> p k n", p=P)).then_inc(w2_loaded, 16)
            with sp.Fori(1, NT // 2) as i:
                for s in range(2):
                    sp.wait_ge(tile_transposed, 2 * i + s - 1)
                    sp.dma_start(idx[:, s, :], ids_t[:, 2 * i + s, :]).then_inc(idx_loaded[s], 16)
                    load_dense(2 * i + s, s)
            sp.wait_ge(y_copied, NT)
            sp.dma_start(out.rearrange("b o -> o b"), y[:].rearrange("o p t -> o (p t)")).then_inc(y_stored, 16)
            sp.wait_ge(y_stored, 16)

        @block.gpsimd
        def _(pool):
            nc.gpsimd.memset(ident[:], 0.0).then_inc(ident_zero, 1)
            nc.gpsimd.iota(row_no[:], [[1, R]], base=0, channel_multiplier=R,
                           allow_small_or_imprecise_dtypes=True).then_inc(row_no_ready, 1)
            nc.gpsimd.iota(row_neg[:], [[-1, R]], base=0, channel_multiplier=-R,
                           allow_small_or_imprecise_dtypes=True).then_inc(row_no_ready, 1)
            pool.wait_ge(ident_zero, 1)
            nc.gpsimd.affine_select(out=ident[:], in_=ident[:], compare_op=ALU.not_equal, fill=1.0, base=0,
                                    pattern=[[-1, P]], channel_multiplier=1).then_inc(ident_ready, 1)

            def gather(s, ids_of_tile):
                for g, vs in enumerate(GROUPS):
                    for v in vs:
                        if v:
                            nc.gpsimd.indirect_dma_start(
                                vecs[:, s, v, :], None, tables[v - 1],
                                bass.IndirectOffsetOnAxis(ids_of_tile[:, v - 1:v], 0)).then_inc(gathered[s][g], 16)

            pool.wait_ge(ids_all_loaded, 16)
            for s in range(2):
                gather(s, ids_all[:, s, :])
            with pool.Fori(1, NT // 2) as i:
                for s in range(2):
                    pool.wait_ge(tile_transposed, 2 * i + s - 1)
                    pool.wait_ge(idx_loaded[s], 16 * i)
                    gather(s, idx[:, s, :])

        def copy_out(e, eng, copy, relu):

            def transposes(i, s, groups):
                for g in groups:
                    if g % 2 != e:
                        continue
                    eng.wait_ge(tp_full[e], GPE * (2 * i + s) + g // 2 + 1)
                    if g == 0:
                        copy(denseT[:, s, :], tp_bank[0][:, 0:P])
                    for n, v0, nv in runs(GROUPS[g]):
                        last = copy(vecsT[:, s, :, v0:v0 + nv],
                                    tp_bank[g][:, n * P:(n + nv) * P].rearrange("d (v b) -> d b v", v=nv))
                        lo, hi = max(v0, DUP), min(v0 + nv, DUP + ND)
                        if lo < hi:
                            last = copy(vecsT[:, s, :, NV + lo - DUP:NV + hi - DUP],
                                        tp_bank[g][:, (n + lo - v0) * P:(n + hi - v0) * P].rearrange(
                                            "d (v b) -> d b v", v=hi - lo))
                    last.then_inc(tp_copied[e], 1)

            def products(i, s):
                for ch in range(NCH):
                    eng.wait_ge(gram_full, NCH * (2 * i + s) + ch + 1)

                    def fill(j, k, rows, c0):
                        src = gram[QUAD * j:QUAD * j + rows, BUFFER[ch], :, 0:BG * GS * NV].rearrange(
                            "r a (q j c) -> r j a q c", q=BG, j=GS)[:, j, :, :, c0:c0 + ZC]
                        dst = Z[QUAD * k:QUAD * k + rows, :, CH * ch:CH * (ch + 1)].rearrange(
                            "r c (a q j) -> r j a q c", q=BG, j=GS)[:, j]
                        return copy(dst, src)

                    for j in (2 * e, 2 * e + 1):
                        for k in range(4):
                            last = fill(j, k, QUAD, QUADS[k][2])
                        last.then_inc(lower_filled[e], 1)
                    for j in (2 * e, 2 * e + 1):
                        eng.wait_ge(lower_filled[e], 2 * (NCH * (2 * i + s) + ch) + j - 2 * e + 1)
                        for k in range(4):
                            last = fill(j, k, *QUADS[k][:2])
                    last.then_inc(gram_copied[e], 1)

            def layer1(i, s):
                eng.wait_ge(l1_full[e], 2 * i + s + 1)
                for n in (2 * e, 2 * e + 1):
                    last = relu(h1[:, n, :], mlp[:, e, (n % 2) * P:(n % 2 + 1) * P], cols[:, n:n + 1])
                last.then_inc(h1_ready[e], 1)

            def layer2(i, s):
                eng.wait_ge(l2_full[e], 2 * i + s + 1)
                relu(h2[:, e, :], l2_acc[e], cols[:, N1T + e:N1T + e + 1]).then_inc(h2_ready[e], 1)

            return transposes, products, layer1, layer2

        @block.vector
        def _(dve):
            def relu(dst, src, bias):
                return nc.vector.tensor_scalar(dst, src, bias, 0.0, ALU.add, ALU.max)

            transposes, products, layer1, layer2 = copy_out(0, dve, nc.vector.tensor_copy, relu)

            nc.vector.memset(zeros[:], 0.0).then_inc(zeros_ready, 1)
            dve.wait_ge(zeros_ready, 1)
            for g in range(ZC):
                if g == ZC // 2:
                    dve.wait_ge(ids_all_loaded, 16)
                    nc.vector.tensor_copy(idsf[:], ids_all[:]).then_inc(idsf_ready, 1)
                    dve.wait_ge(ident_ready, 1)
                    nc.vector.tensor_copy(ident_r[:], ident[0:F, 0:F]).then_inc(idsT_ready, 1)
                last = nc.vector.tensor_copy(Wz[:, g, :], zeros[:])
            last.then_inc(wz_zeroed, 1)
            dve.wait_ge(idsT_full, 1)
            nc.vector.tensor_copy(idsT[:], mlp[0:F, 0, :]).then_inc(idsT_ready, 1)
            dve.wait_ge(row_no_ready, 2)
            for u in range(NPK):
                dve.wait_ge(wanted_ready, u + 1)
                if u >= 2:
                    dve.wait_ge(selected, u - 1)
                for r in range(R - ON_ACT[u]):
                    nc.vector.tensor_scalar(onehot[:, u % 2, r, :], wanted[:, u, :], row_no[0:KP, r:r + 1],
                                            None, ALU.is_equal).then_inc(onehot_dve, 1)
                dve.wait_ge(hi_ready, u + 1)
                nc.vector.tensor_tensor(tab_lo[:, u % 2], table[:, u], tab_hi[:, u % 3].bitcast(F32),
                                        ALU.subtract).then_inc(lo_ready, 1)
                if u == 3:
                    dve.wait_ge(cols_full, 1)
                    nc.vector.tensor_copy(cols[:], gram[:, 0, 0, 0:NR]).then_inc(cols_ready, 1)
                if u >= 1:
                    transposes(0, 0, SETUP_GROUPS[u - 1])
            dve.wait_ge(wd_loaded, 32)
            nc.vector.tensor_tensor(Wd[:], Wda[:], Wdb[:], ALU.add).then_inc(wd_ready, 1)
            transposes(0, 0, SETUP_GROUPS[NPK - 1])

            def keep_y(t):
                dve.wait_ge(l3_full, t + 1)
                if not isinstance(t, int):
                    t = nc.s_assert_within(t, 0, NT - 1)
                nc.vector.tensor_copy(y[:, :, bass.ds(t, 1)].rearrange("o p t -> o (p t)"),
                                      l3_acc).then_inc(y_copied, 1)

            with dve.Fori(0, NT // 2) as i:
                for s in range(2):
                    products(i, s)
                    with if_next(dve, i, s):
                        transposes(*after(i, s), [0, 2])
                    with if_prev(dve, i, s):
                        keep_y(2 * i + s - 1)
                    layer1(i, s)
                    with if_next(dve, i, s):
                        transposes(*after(i, s), [4])
                    layer2(i, s)
            keep_y(NT - 1)

        @block.scalar
        def _(act):
            def relu(dst, src, bias):
                return nc.scalar.activation(dst, src, ACT.Relu, bias=bias)

            transposes, products, layer1, layer2 = copy_out(1, act, nc.scalar.copy, relu)

            def place_picked(i, s, u):
                first = (2 * i + s) * P if isinstance(i, int) else nc.s_assert_within((2 * i + s) * P, 0, B - P)
                nc.scalar.copy(vecsT[:, s, :, picks[u]], picked[:, u, bass.ds(first, P)])

            act.wait_ge(zeros_ready, 1)
            for s in range(2):
                pad = QUAD - len(ROWS)
                last = nc.scalar.copy(vecsT[:, s, :, len(ROWS):QUAD],
                                      zeros[:, 0:P * pad].rearrange("p (b v) -> p b v", v=pad))
            last.then_inc(pad_zeroed, 1)
            act.wait_ge(row_no_ready, 2)

            def spread(u):
                act.wait_ge(ids_spread, u + 1)
                nc.scalar.copy(wanted[:, u, :], spread_ids[u][0:KP]).then_inc(wanted_ready, 1)

            def high_part(u):
                act.wait_ge(table_loaded[u], 16)
                nc.scalar.copy(tab_hi[:, u % 3], table[:, u]).then_inc(hi_ready, 1)

            def one_hot(u):
                if u >= 2:
                    act.wait_ge(selected, u - 1)
                act.wait_ge(wanted_ready, u + 1)
                rs = range(R - ON_ACT[u], R)
                for r in rs:
                    nc.scalar.activation(onehot[:, u % 2, r, :], wanted[:, u, :], ACT.Abs,
                                         bias=row_neg[0:KP, r:r + 1]).then_inc(apart_ready, 1)
                for n, r in enumerate(rs):
                    act.wait_ge(apart_ready, made(u, True) + n + 1)
                    nc.scalar.activation(onehot[:, u % 2, r, :], onehot[:, u % 2, r, :].bitcast(F32), ACT.Relu,
                                         bias=1.0, scale=-1.0).then_inc(onehot_act, 1)

            def keep_picked(u):
                act.wait_ge(selected, u + 1)
                nc.scalar.copy(picked[:, u, :], mlp[:, (NPK - u) % 2, :]).then_inc(picked_ready, 1)

            high_part(0)
            for u in (0, 1):
                spread(u)
            for u in range(NPK):
                one_hot(u)
                if u + 1 < NPK:
                    high_part(u + 1)
                for later in range(2 * u + 2, min(2 * u + 4, NPK)):
                    spread(later)
                if u >= 1:
                    keep_picked(u - 1)
                    act.wait_ge(picked_ready, u)
                    place_picked(0, 0, u - 1)
                    transposes(0, 0, SETUP_GROUPS[u - 1])
            transposes(0, 0, SETUP_GROUPS[NPK - 1])
            act.wait_ge(cols_ready, 1)
            act.wait_ge(selected, NPK)
            nc.scalar.copy(vecsT[:, 0, :, picks[-1]], mlp[:, 1, 0:P]).then_inc(last_placed, 1)
            keep_picked(NPK - 1)

            with act.Fori(0, NT // 2) as i:
                for s in range(2):
                    products(i, s)
                    with if_next(act, i, s):
                        transposes(*after(i, s), [1])
                        for u in range(NPK):
                            place_picked(*after(i, s), u)
                    layer1(i, s)
                    with if_next(act, i, s):
                        transposes(*after(i, s), [3, 5])
                    layer2(i, s)

        @block.tensor
        def _(pe):
            def transposes(i, s, groups):
                t = 2 * i + s
                for g in groups:
                    e = g % 2
                    if g < 4 and not isinstance(i, int):
                        for half in range(2):
                            pe.wait_ge(gram_copied[half], NCH * (t - 1) + (3 if g >= 2 else 2))
                    if g == 0:
                        pe.wait_ge(dense_loaded[s], 16 * (i + 1))
                    pe.wait_ge(gathered[s][g], 16 * (len(GROUPS[g]) - (g == 0)) * (i + 1))
                    for n, v in enumerate(GROUPS[g]):
                        last = nc.tensor.transpose(tp_bank[g][:, n * P:(n + 1) * P], vecs[:, s, v, :], ident[:])
                    last.then_inc(tp_full[e], 1)

            def dense_layer1(s, e):
                for n in (2 * e, 2 * e + 1):
                    nc.tensor.matmul(mlp[:, n // 2, (n % 2) * P:(n % 2 + 1) * P], Wd[:, n * P:(n + 1) * P],
                                     denseT[:, s, :], start=(n % 2 == 0), stop=False, skip_group_check=True)

            def products(i, s):
                t = 2 * i + s
                for e in range(2):
                    pe.wait_ge(tp_copied[e], GPE * (t + 1))
                for ch in range(NCH):
                    if ch in (1, 2):
                        with if_prev(pe, i, s):
                            pe.wait_ge(h2_ready[ch % 2], t)
                    if ch == 3:
                        for e in range(2):
                            pe.wait_ge(gram_copied[e], NCH * t + 1)
                    for m in range(CH // GS):
                        b = CH * ch + GS * m
                        o = (m % BG) * GS * NV
                        last = nc.tensor.matmul(
                            gram[:, BUFFER[ch], m // BG, o:o + GS * NV],
                            vecsT[:, s, b:b + GS, :].rearrange("d b v -> d (b v)"),
                            vecsT[:, s, b:b + GS, 0:NV], start=True, stop=True)
                        if ch == 0 and m == 0:
                            last.then_inc(tile_transposed, 1)
                    last.then_inc(gram_full, 1)

            def layer1(i, s):
                t = 2 * i + s
                for e in range(2):
                    pe.wait_ge(gram_copied[e], NCH * (t + 1))
                pe.wait_ge(wz_loaded, 16 * len(wz_parts()))
                for n in range(N1T):
                    for g in range(ZC):
                        last = nc.tensor.matmul(mlp[:, n // 2, (n % 2) * P:(n % 2 + 1) * P],
                                                Wz[:, g, n * P:(n + 1) * P], Z[:, g, :], start=False,
                                                stop=(g == ZC - 1), skip_group_check=True)
                    if n % 2:
                        last.then_inc(l1_full[n // 2], 1)

            def layer2(i, s, half):
                pe.wait_ge(w2_loaded, 16)
                pe.wait_ge(h1_ready[half], 2 * i + s + 1)
                for e in range(N2T):
                    for n in (2 * half, 2 * half + 1):
                        last = nc.tensor.matmul(l2_acc[e], W2s[:, n, e * P:(e + 1) * P], h1[:, n, :],
                                                start=(n == 0), stop=(n == N1T - 1))
                    if half:
                        last.then_inc(l2_full[e], 1)

            def layer3(t):
                for e in range(N2T):
                    pe.wait_ge(h2_ready[e], t + 1)
                    last = nc.tensor.matmul(l3_acc, cols[:, N1T + N2T + e:N1T + N2T + e + 1],
                                            h2[:, e, :], start=(e == 0), stop=(e == N2T - 1))
                last.then_inc(l3_full, 1)

            pe.wait_ge(ident_ready, 1)
            pe.wait_ge(idsf_ready, 1)
            for t in range(NT):
                last = nc.tensor.transpose(mlp[0:F, 0, t * P:(t + 1) * P], idsf[:, t, :], ident[:])
            last.then_inc(idsT_full, 1)
            pe.wait_ge(idsT_ready, 2)

            def spread(u):
                v = picks[u]
                if u >= 6:
                    pe.wait_ge(wanted_ready, u - 5)
                nc.tensor.matmul(spread_ids[u], ident_r[:, v - 1:v].to_broadcast([F, P]), idsT[:],
                                 start=True, stop=True).then_inc(ids_spread, 1)

            for u in range(4):
                spread(u)
            for u in range(NPK):
                if u >= 2:
                    pe.wait_ge(picked_ready, u - 1)
                pe.wait_ge(hi_ready, u + 1)
                for r in range(R):
                    if r < R - ON_ACT[u]:
                        pe.wait_ge(onehot_dve, made(u, False) + r + 1)
                    else:
                        pe.wait_ge(onehot_act, made(u, True) + r - (R - ON_ACT[u]) + 1)
                    nc.tensor.matmul(mlp[:, (NPK - u) % 2, :], tab_hi[:, u % 3, r, :], onehot[:, u % 2, r, :],
                                     start=(r == 0), stop=False)
                pe.wait_ge(lo_ready, u + 1)
                for r in range(R):
                    last = nc.tensor.matmul(mlp[:, (NPK - u) % 2, :], tab_lo[:, u % 2, r, :], onehot[:, u % 2, r, :],
                                            start=False, stop=(r == R - 1))
                last.then_inc(selected, 1)
                if u == 0:
                    for later in range(4, NPK):
                        spread(later)
                if u == 2:
                    pe.wait_ge(wanted_ready, NPK)
                    pe.wait_ge(rows_loaded, 48)
                    nc.tensor.transpose(gram[:, 0, 0, 0:NR], rows[:], ident[0:NR, 0:NR]).then_inc(cols_full, 1)
                if u == 3:
                    pe.wait_ge(cols_ready, 1)
                transposes(0, 0, SETUP_GROUPS[u])
            pe.wait_ge(wd_ready, 1)
            pe.wait_ge(picked_ready, NPK - 1)
            dense_layer1(0, 0)
            pe.wait_ge(pad_zeroed, 1)
            pe.wait_ge(last_placed, 1)

            with pe.Fori(0, NT // 2) as i:
                for s in range(2):
                    products(i, s)
                    with if_next(pe, i, s):
                        transposes(*after(i, s), [0, 1, 2])
                    with if_prev(pe, i, s):
                        for e in range(2):
                            pe.wait_ge(gram_copied[e], NCH * (2 * i + s) + 3)
                        layer3(2 * i + s - 1)
                    dense_layer1(s, 1)
                    layer1(i, s)
                    with if_next(pe, i, s):
                        pe.wait_ge(h1_ready[0], 2 * i + s + 1)
                        transposes(*after(i, s), [3])
                    layer2(i, s, 0)
                    with if_next(pe, i, s):
                        transposes(*after(i, s), [4])
                    layer2(i, s, 1)
                    with if_next(pe, i, s):
                        transposes(*after(i, s), [5])
                        dense_layer1(1 - s, 0)
            layer3(NT - 1)


_TABLES = [f'tbl_{f}' for f in range(26)]
_INS = ['r_dense_features', 'ids'] + _TABLES + ['W_top1', 'b_top1', 'W_top2', 'b_top2', 'W_top3']


def kernel(**inputs):
    import numpy as np
    import concourse.bacc as bacc
    from concourse.bass_utils import run_bass_kernel_spmd

    nc = bacc.Bacc("TRN2", target_bir_lowering=False, num_devices=1)
    arrays, aps = {}, {}
    for name in _INS:
        a = np.ascontiguousarray(inputs[name])
        arrays[f"in_{name}_dram"] = a
        aps[name] = nc.dram_tensor(f"in_{name}_dram", a.shape, mybir.dt.from_np(a.dtype), kind="ExternalInput").ap()
    out = nc.dram_tensor("out_0_dram", (aps['ids'].shape[0], 1), F32, kind="ExternalOutput").ap()
    dlrm_tower_kernel(nc, aps['r_dense_features'], aps['ids'], [aps[t] for t in _TABLES], aps['W_top1'],
                      aps['b_top1'], aps['W_top2'], aps['b_top2'], aps['W_top3'], out)
    r = run_bass_kernel_spmd(nc, [arrays], core_ids=[0])
    return r.results[0]["out_0_dram"]
```
